# Optimizing a Trainium2 kernel written in Bass

```python
import numpy as np
import jax
import jax.numpy as jnp

def _softmax(x, axis=-1):
    return jax.nn.softmax(x, axis=axis)

def _gelu(x):
    return jax.nn.gelu(x, approximate=True)

def _silu(x):
    return jax.nn.silu(x)

def _sigmoid(x):
    return jax.nn.sigmoid(x)

def _layernorm(x, axis=-1, eps=1e-05):
    m = jnp.mean(x, axis=axis, keepdims=True)
    v = jnp.var(x, axis=axis, keepdims=True)
    return (x - m) / jnp.sqrt(v + eps)

def _scatter_add(tgt, idx, src, axis=0):
    return tgt.at[idx].add(src)

def _segment_sum(src, seg, n):
    return jax.ops.segment_sum(src, seg, n)
kernel_name = 'mk_rec_standalone_d1_rec_r8_418a83'

def setup_inputs(seed: int=0):
    np.random.seed(seed)
    _w = jnp.asarray

    def _rec_inputs():
        import jax
        import jax.numpy as jnp
        _rk = jax.random.key(seed)
        r_x = 8.71811e-05 + 1.00005 * jax.random.normal(jax.random.fold_in(_rk, 1), (2048, 39, 16), jnp.float32)
        return r_x
    r_x = _rec_inputs()

    def _L0_rec_setup():
        import jax, jax.numpy as jnp
        import numpy as np
        B, F, D = (1024, 39, 16)
        HIDDEN = [128, 128, 128]

        def _cin(x, Ws, bs):
            F0 = x.shape[1]
            h = x
            outs = []
            n = len(Ws)
            for i, (W, b) in enumerate(zip(Ws, bs)):
                L = W.shape[-1]
                Fk = h.shape[1]
                Wr = W.reshape(F0, Fk, L)
                z = jnp.einsum('bfd,bgd->bfgd', x, h)
                cur = jax.nn.relu(jnp.einsum('bfgd,fgl->bld', z, Wr) + b[None, :, None])
                if i != n - 1:
                    h = cur[:, :L // 2]
                    direct = cur[:, L // 2:]
                else:
                    direct = cur
                outs.append(direct)
            return jnp.concatenate(outs, axis=1).sum(-1)
        key = jax.random.key(seed)
        ks = jax.random.split(key, 8)
        x = jax.random.normal(ks[0], (B, F, D), dtype=jnp.float32)
        field_nums = [F]
        Ws, bs = ([], [])
        for i, L in enumerate(HIDDEN):
            fan_in = field_nums[0] * field_nums[-1]
            lim = np.sqrt(6.0 / fan_in)
            Ws.append(jax.random.uniform(ks[1 + i], (fan_in, L), jnp.float32, -lim, lim))
            bs.append(jnp.zeros((L,), jnp.float32))
            field_nums.append(L // 2)
        return {'x': x, 'W0': Ws[0], 'W1': Ws[1], 'W2': Ws[2], 'b0': bs[0], 'b1': bs[1], 'b2': bs[2]}
    _L0_rec_all = _L0_rec_setup()
    _L0_rec_in = {k: v for k, v in _L0_rec_all.items() if k in ('W0', 'W1', 'W2', 'b0', 'b1', 'b2')}
    del _L0_rec_all
    return {'r_x': r_x, 'L0_rec_W0': _L0_rec_in['W0'], 'L0_rec_W1': _L0_rec_in['W1'], 'L0_rec_W2': _L0_rec_in['W2'], 'L0_rec_b0': _L0_rec_in['b0'], 'L0_rec_b1': _L0_rec_in['b1'], 'L0_rec_b2': _L0_rec_in['b2']}

def reference(r_x, L0_rec_W0, L0_rec_W1, L0_rec_W2, L0_rec_b0, L0_rec_b1, L0_rec_b2):
    import jax
    import jax.numpy as jnp

    def _L0_rec_ref(x, W0, W1, W2, b0, b1, b2):
        import jax, jax.numpy as jnp
        import numpy as np
        B, F, D = (1024, 39, 16)
        HIDDEN = [128, 128, 128]

        def _cin(x, Ws, bs):
            F0 = x.shape[1]
            h = x
            outs = []
            n = len(Ws)
            for i, (W, b) in enumerate(zip(Ws, bs)):
                L = W.shape[-1]
                Fk = h.shape[1]
                Wr = W.reshape(F0, Fk, L)
                z = jnp.einsum('bfd,bgd->bfgd', x, h)
                cur = jax.nn.relu(jnp.einsum('bfgd,fgl->bld', z, Wr) + b[None, :, None])
                if i != n - 1:
                    h = cur[:, :L // 2]
                    direct = cur[:, L // 2:]
                else:
                    direct = cur
                outs.append(direct)
            return jnp.concatenate(outs, axis=1).sum(-1)
        return _cin(x, [W0, W1, W2], [b0, b1, b2])
    y = _L0_rec_ref(r_x, L0_rec_W0, L0_rec_W1, L0_rec_W2, L0_rec_b0, L0_rec_b1, L0_rec_b2)
    return y

_drawn_inputs = setup_inputs


def setup_inputs(seed=0):
    import zlib

    import numpy as np

    out = dict(_drawn_inputs(seed))
    spreads = {'L0_rec_b0': (0.0, 0.1), 'L0_rec_b1': (0.0, 0.1), 'L0_rec_b2': (0.0, 0.1)}
    factors = {}
    for name, (base, spread) in spreads.items():
        noise = np.random.default_rng([zlib.crc32(name.encode()), seed]).standard_normal(out[name].shape)
        drawn = base * np.exp(spread * noise) if base else spread * noise
        out[name] = jnp.asarray(drawn.astype(out[name].dtype))
    for name, factor in factors.items():
        out[name] = (out[name] * factor).astype(out[name].dtype)
    return out
```

```python
import concourse.bass as bass
from concourse import mybir
from contextlib import ExitStack

F = 39
D = 16
B = 2048
L = 128
H = L // 2
NCOL = 512
BB = NCOL // D
NBLK = B // BB
KS = 3
P0 = KS * F
T0 = 7
K0_LAST = (20 - KS * (T0 - 1)) * F
T1 = (F + 1) // 2
XP = 64 + F

G0, G1 = 4, T1 // 2
SLOTS = list(range(2 * G1 + G0))
S_L0, S_L2 = G1, G1 + G0
LAST_SLOTS = [s for s in SLOTS if not S_L0 <= s < S_L2]
FIRST_SLOTS = [s for s in SLOTS if S_L0 <= s < S_L2]
RING = 6
SUB_DVE = [2, 4, 6, 8, 11, 16, 18, 20, 22]
SUB_POOL = [1, 3, 5, 7, 9, 12, 13, 15, 17, 19, 21, 23]
SPLIT = sorted(SUB_DVE + SUB_POOL)
WHOLE = [s for s in SLOTS if s not in SPLIT and not S_L0 <= s < S_L2]
NBC = G0 + G1
BC_AFTER = [4, 5, 6, 7] + [12 + j for j in range(G1)]
SUB_LAG = 2
ACT_EVAC_AT = [[], [], [], [], [], [], [], [0], [], [], [], [], [], [], [],
               [4], [5], [6], [7], [8], [9], [10], [11], [12, 13]]
ACT_RELU_L2_AT, ACT_X_AT, ACT_RELU_L1_AT, ACT_RELU_L0_AT = 3, 9, 13, 17
DVE_SUM_L2_AT, DVE_SUM_L1_AT = 6, 18
POOL_X_AT = 11


def executed(slots, c, s):
    first = len([p for p in slots if p in FIRST_SLOTS])
    upto = len([p for p in slots if p <= s])
    if isinstance(c, int) and c == -1:
        return len([p for p in slots if p in FIRST_SLOTS and p <= s])
    skipped = first if isinstance(c, int) and c == NBLK - 1 and s >= S_L2 else 0
    return c * len(slots) + (first + upto - skipped)


def place(s, last):
    return (len(FIRST_SLOTS) + s - (G0 if last and s >= S_L2 else 0)) % RING


def tiles_of(s):
    if s < S_L0:
        return [2 * s, 2 * s + 1]
    if s < S_L2:
        g = s - S_L0
        return [0] if g == 0 else [2 * g - 1, 2 * g]
    return [2 * (s - S_L2), 2 * (s - S_L2) + 1]


def build(nc, x_t, w0a_d, w0b_d, w1_d, w2_d, eye_d, b0_d, b1_d, b2_d, y_d):
    fp32 = mybir.dt.float32
    f32r = mybir.dt.float32r
    ALU = mybir.AluOpType
    ACT = mybir.ActivationFunctionType
    AX = mybir.AxisListType

    with ExitStack() as ctx:
        def sb(name, shape, dt=fp32):
            return ctx.enter_context(nc.sbuf_tensor(name, shape, dt))

        def sem(name):
            return ctx.enter_context(nc.semaphore(name))

        w0_f = sb("w0_f", [P0, T0, L])
        w12_f = sb("w12_f", [128, len(WHOLE), 2, L])
        w_h = [sb("w0_h", [P0, T0, L], f32r), sb("w1_h", [128, T1, L], f32r), sb("w2_h", [128, T1, L], f32r)]
        w_l = [sb("w0_l", [P0, T0, L], f32r), sb("w1_l", [128, T1, L], f32r), sb("w2_l", [128, T1, L], f32r)]
        eye = sb("eye", [XP, 2 * F + 1])
        pick0 = sb("pick0", [XP, T0 + 1, P0], f32r)
        pick1 = sb("pick1", [XP, T1, 128], f32r)
        bias = sb("bias", [128, 3])

        x_in = sb("x_in", [XP, 2, NCOL])
        x_split = sb("x_split", [XP, 2, NCOL], f32r)
        x_rep = sb("x_rep", [P0, NCOL])
        x_bc = sb("x_bc", [128, T1, NCOL])
        stage = x_bc[:, :, :].rearrange("p t n -> p (t n)")
        at0, at1, at2 = (T1 - 12) * NCOL, (T1 - 10) * NCOL, (T1 - 5) * NCOL
        w0_mirror = stage[0:P0, at0:at0 + T0 * L].rearrange("p (t l) -> p t l", l=L)
        w_full = [w0_f[:, :, :],
                  stage[:, at1:at1 + T1 * L].rearrange("p (t l) -> p t l", l=L),
                  stage[:, at2:at2 + T1 * L].rearrange("p (t l) -> p t l", l=L)]
        z = sb("z", [128, RING, 2, NCOL])
        z_h = sb("z_h", [128, RING, 2, NCOL], f32r)
        z_l = sb("z_l", [128, RING, 2, NCOL], f32r)
        direct01 = sb("direct01", [128, 2, NCOL])
        direct2 = sb("direct2", [128, NCOL])
        y_sum = sb("y_sum", [128, 2, 2, BB])

        acc = [ctx.enter_context(nc.psum_tensor(f"acc{i}", [128, NCOL], fp32)) for i in range(2)]
        h = [ctx.enter_context(nc.psum_tensor(f"h{i}", [128, NCOL], fp32)) for i in range(2)]
        bc = [ctx.enter_context(nc.psum_tensor(f"bc{i}", [128, 2, NCOL], fp32)) for i in range(2)]

        w0_loaded, w1_loaded, w2_loaded = sem("w0_loaded"), sem("w1_loaded"), sem("w2_loaded")
        w12_whole_loaded, eye_loaded, bias_loaded = sem("w12_whole_loaded"), sem("eye_loaded"), sem("bias_loaded")
        x_cleared = sem("x_cleared")
        w0_summed = sem("w0_summed")
        w_high = sem("w_high")
        w_low = sem("w_low")
        picks_made = sem("picks_made")
        x_loaded = [sem("x_loaded_even"), sem("x_loaded_odd")]
        x_high = sem("x_high")
        x_low = sem("x_low")
        spread = sem("spread")
        evacuated = sem("evacuated")
        h_ready = sem("h_ready")
        acc_drained = sem("acc_drained")
        z_made = sem("z_made")
        zh_made = sem("zh_made")
        zl_dve = sem("zl_dve")
        zl_pool = sem("zl_pool")
        contracted = sem("contracted")
        summed = sem("summed")
        y_stored = [sem("y_stored_even"), sem("y_stored_odd")]

        block = ctx.enter_context(nc.Block())

        def load_x(eng, b, par, used):
            if used:
                eng.wait_ge(x_low, b - 1)
            src = x_t[:, bass.ds(b * NCOL, NCOL)]
            eng.dma_start(x_in[0:F, par, :], src).then_inc(x_loaded[par], 16)
            eng.dma_start(x_in[64:XP, par, :], src).then_inc(x_loaded[par], 16)

        def store_y(eng, c, par):
            eng.wait_ge(summed, 2 * c + 2)
            dst = y_d[:, :, bass.ds(c * BB, BB)].rearrange("a p b -> p a b")
            eng.dma_start(dst, y_sum[:, par, :, :]).then_inc(y_stored[par], 16)

        @block.sync
        def _(sp):
            sp.dma_start(eye[:, :], eye_d).then_inc(eye_loaded, 16)
            sp.wait_ge(x_cleared, 1)
            load_x(sp, 0, 0, False)
            load_x(sp, 1, 1, False)
            sp.dma_start(w_full[1], w1_d).then_inc(w1_loaded, 16)
            for n, s in enumerate(WHOLE):
                w_d, t = (w1_d if s < S_L0 else w2_d), tiles_of(s)[0]
                sp.dma_start(w12_f[:, n, :, :], w_d[:, t:t + 2, :]).then_inc(w12_whole_loaded, 16)
            sp.dma_start(w_full[2], w2_d).then_inc(w2_loaded, 16)

            def pair(c, last=False):
                for par in range(2):
                    if not last:
                        load_x(sp, c + par + 2, par, True)
                    store_y(sp, c + par, par)

            with sp.Fori(0, NBLK // 2 - 1) as i:
                pair(2 * i)
            pair(NBLK - 2, last=True)
            sp.wait_ge(y_stored[0], 16 * (NBLK // 2))
            sp.wait_ge(y_stored[1], 16 * (NBLK // 2))

        def pe_spread(pe, k, c, par, free):
            if k == 0:
                pe.wait_ge(x_low, c + 2)
            if free == "loop":
                if k < 2:
                    pe.wait_ge(evacuated, (c + 1) * (G1 + 1) - 1 + k)
                if k == 2:
                    pe.wait_ge(evacuated, (c + 1) * (G1 + 1) + 1)
            if k in (2, 3, 4, 5):
                pe.wait_ge(z_made, executed(SLOTS, c, S_L0 + k - 2))
            if free == "first" and k == 2:
                pe.wait_ge(evacuated, 1)
            if k >= 6:
                pe.wait_ge(evacuated, (c + 1) * (G1 + 1) + 1 + k - 5)
            xs = x_split[:, par, :]
            out = bc[k % 2]
            if k == 0:
                for a in range(2):
                    last = nc.tensor.matmul(out[0:P0, a, :], pick0[:, a, :], xs, start=True, stop=True)
            elif k < G0:
                for a, t in enumerate(tiles_of(S_L0 + k)):
                    last = nc.tensor.matmul(out[0:P0, a, :], pick0[:, 1 + t, :], xs, start=True, stop=True)
            else:
                for a, t in enumerate(tiles_of(k - G0)):
                    last = nc.tensor.matmul(out[:, a, :], pick1[:, t, :], xs, start=True, stop=True)
            last.then_inc(spread, 1)

        def pe_contract(pe, c, par, s, last):
            layer = 1 if s < S_L0 else 0 if s < S_L2 else 2
            stage = 3 * c + (1 if layer == 1 else 2 if layer == 0 or last else 3)
            a = acc[(par + (1 if layer == 1 else 0 if layer == 0 or last else 1)) % 2]
            tiles = tiles_of(s)
            n_tiles = T0 if layer == 0 else T1
            if tiles[0] == 0 and not (isinstance(stage, int) and stage < 2):
                pe.wait_ge(acc_drained, stage - 1)
            slot = place(s, last)
            kp = [K0_LAST if layer == 0 and t == T0 - 1 else P0 if layer == 0 else 128 for t in tiles]
            if s not in SPLIT:
                pe.wait_ge(z_made, executed(SLOTS, c, s))
                for j, t in enumerate(tiles):
                    w = w0_f[0:kp[j], t, :] if layer == 0 else w12_f[:, WHOLE.index(s), j, :]
                    m = nc.tensor.matmul(a[:, :], w, z[0:kp[j], slot, j, :],
                                         start=(t == 0), stop=(t == n_tiles - 1))
            else:
                pe.wait_ge(zh_made, executed(SPLIT, c, s))
                for j, t in enumerate(tiles):
                    for w in (w_h, w_l):
                        m = nc.tensor.matmul(a[:, :], w[layer][0:kp[j], t, :], z_h[0:kp[j], slot, j, :],
                                             start=(t == 0 and w is w_h), stop=False)
                if s in SUB_DVE:
                    pe.wait_ge(zl_dve, executed(SUB_DVE, c, s))
                else:
                    pe.wait_ge(zl_pool, executed(SUB_POOL, c, s))
                for j, t in enumerate(tiles):
                    m = nc.tensor.matmul(a[:, :], w_h[layer][0:kp[j], t, :], z_l[0:kp[j], slot, j, :],
                                         start=False, stop=(t == n_tiles - 1))
            m.then_inc(contracted, 1)

        @block.tensor
        def _(pe):
            pe.wait_ge(picks_made, 2)
            for k in range(G0):
                pe_spread(pe, k, -1, 0, "first")
            pe.wait_ge(w_high, 1)
            pe.wait_ge(w_low, 1)
            for s in FIRST_SLOTS:
                pe_contract(pe, -1, 1, s, False)
            pe.wait_ge(picks_made, 3)
            for k in range(G0, NBC):
                pe_spread(pe, k, -1, 0, "first")

            def pair(c, free="loop", last=False):
                for par in range(2):
                    end = last and par == 1
                    for s in (LAST_SLOTS if end else SLOTS):
                        if free == "first" and par == 0 and s == 0:
                            pe.wait_ge(w12_whole_loaded, 16 * len(WHOLE))
                        if free == "first" and par == 0 and s in (0, S_L2):
                            pe.wait_ge(w_high, 2 if s == 0 else 3)
                            pe.wait_ge(w_low, 2 if s == 0 else 3)
                        pe_contract(pe, c + par, par, s, end)
                        for k in range(NBC):
                            if BC_AFTER[k] == s and not end:
                                pe_spread(pe, k, c + par, (par + 1) % 2, "loop")

            pair(0, free="first")
            with pe.Fori(1, NBLK // 2 - 1) as i:
                pair(2 * i)
            pair(NBLK - 2, last=True)

        def act_split_x(act, b, par, used):
            act.wait_ge(x_loaded[par], 32 * ((b - par) // 2 + 1) if isinstance(b, int) else used)
            nc.scalar.activation(x_split[:, par, :], x_in[:, par, :], ACT.Copy).then_inc(x_high, 1)

        def act_evac(act, c, k):
            act.wait_ge(spread, (c + 1) * NBC + k + 1)
            if k == 0:
                nc.scalar.activation(x_rep[:, :], bc[0][0:P0, 0, :], ACT.Copy).then_inc(evacuated, 1)
            else:
                g = k - G0
                if not (isinstance(c, int) and c == -1):
                    act.wait_ge(z_made, executed(SLOTS, c, S_L2 + g))
                elif g == T1 // 2 - 6:
                    act.wait_ge(w_low, 3)
                nc.scalar.activation(x_bc[:, 2 * g:2 * g + 2, :], bc[k % 2][:, :, :], ACT.Copy).then_inc(evacuated, 1)

        def act_round(act, c, s, last):
            if s not in SPLIT:
                return
            act.wait_ge(z_made, executed(SLOTS, c, s))
            slot, n = place(s, last), len(tiles_of(s))
            p = P0 if S_L0 <= s < S_L2 else 128
            nc.scalar.activation(z_h[0:p, slot, 0:n, :], z[0:p, slot, 0:n, :], ACT.Copy).then_inc(zh_made, 1)

        def act_relu(act, c, par, layer, last):
            stage = {1: 1, 0: 2, 2: 2 if last else 3}[layer]
            a = acc[(par + stage) % 2]
            end = {1: S_L0 - 1, 0: S_L2 - 1, 2: SLOTS[-1]}[layer]
            act.wait_ge(contracted, executed(SLOTS, c, end))
            blk = (par + 1) % 2 if layer == 0 else par
            if layer < 2:
                for half in range(2):
                    nc.scalar.activation(h[layer][H * half:H * half + H, :], a[0:H, :], ACT.Relu,
                                         bias=bias[0:H, layer:layer + 1]).then_inc(h_ready, 1)
                dst = direct01[H:L, blk, :] if layer == 0 else direct01[0:H, blk, :]
                b = c + 1 if layer == 0 else c
                if not (isinstance(b, int) and b < 2):
                    act.wait_ge(summed, 2 * b - 3)
                nc.scalar.activation(dst, a[H:L, :], ACT.Relu, bias=bias[H:L, layer:layer + 1]).then_inc(acc_drained, 1)
            else:
                if not (isinstance(c, int) and c == 0):
                    act.wait_ge(summed, 2 * c)
                nc.scalar.activation(direct2[:, :], a[:, :], ACT.Relu, bias=bias[:, 2:3]).then_inc(acc_drained, 1)

        @block.scalar
        def _(act):
            act.dma_start(w0_f[:, :, :], w0a_d).then_inc(w0_loaded, 16)
            act.dma_start(w0_mirror, w0b_d).then_inc(w0_loaded, 16)
            for n, b_d in enumerate((b0_d, b1_d, b2_d)):
                act.dma_start(bias[:, n:n + 1], b_d.rearrange("(p a) -> p a", a=1)).then_inc(bias_loaded, 16)
            act.wait_ge(eye_loaded, 16)
            nc.scalar.activation(pick0[:, 0, :].rearrange("p (k f) -> p k f", f=F),
                                 eye[:, 0:F].unsqueeze(1).to_broadcast([XP, KS, F]), ACT.Copy).then_inc(picks_made, 1)
            nc.scalar.activation(pick0[:, 1:T0 + 1, :].rearrange("p t (k f) -> p (t k) f", f=F),
                                 bass.AP(tensor=eye, offset=0, ap=[[2 * F + 1, XP], [1, T0 * KS], [1, F]]),
                                 ACT.Copy).then_inc(picks_made, 1)
            act_split_x(act, 0, 0, None)
            act.wait_ge(w0_summed, 1)
            nc.scalar.activation(w_h[0][:, :, :], w_full[0], ACT.Copy).then_inc(w_high, 1)
            act_evac(act, -1, 0)
            for s in FIRST_SLOTS:
                act_round(act, -1, s, False)
            act_split_x(act, 1, 1, None)
            act.wait_ge(w1_loaded, 16)
            nc.scalar.activation(w_h[1][:, :, :], w_full[1], ACT.Copy).then_inc(w_high, 1)
            act.wait_ge(w2_loaded, 16)
            nc.scalar.activation(w_h[2][:, :, :], w_full[2], ACT.Copy).then_inc(w_high, 1)
            act.wait_ge(bias_loaded, 48)
            act_relu(act, -1, 1, 0, False)
            for k in range(G0, NBC):
                act_evac(act, -1, k)

            def pair(c, first=False, last=False):
                for par in range(2):
                    end = last and par == 1
                    for s in (LAST_SLOTS if end else SLOTS):
                        act_round(act, c + par, s, end)
                        if s == ACT_RELU_L2_AT and not (first and par == 0):
                            act_relu(act, c + par - 1, (par + 1) % 2, 2, False)
                        if s == ACT_X_AT and not last:
                            act_split_x(act, c + par + 2, par, 16 * c + 64)
                        if s == (S_L0 - 1 if end else ACT_RELU_L1_AT):
                            act_relu(act, c + par, par, 1, end)
                        if s == ACT_RELU_L0_AT and not end:
                            act_relu(act, c + par, par, 0, False)
                        for k in ACT_EVAC_AT[s]:
                            if not end:
                                act_evac(act, c + par, k)

            pair(0, first=True)
            with act.Fori(1, NBLK // 2 - 1) as i:
                pair(2 * i)
            pair(NBLK - 2, last=True)
            act_relu(act, NBLK - 1, 1, 2, True)

        def dve_product(dve, c, s, last):
            slot = place(s, last)
            count = executed(SLOTS, c, s)
            if not (isinstance(count, int) and count <= RING):
                dve.wait_ge(contracted, count - RING)
            if s < S_L0 or s >= S_L2:
                layer = 1 if s < S_L0 else 2
                t = tiles_of(s)[0]
                if layer == 1:
                    dve.wait_ge(evacuated, (c + 1) * (G1 + 1) + 1 - (G1 + 1) + s + 1)
                if t == 0:
                    dve.wait_ge(h_ready, 4 * c + 2 if layer == 1 else 4 * c + 4)
                nc.vector.tensor_tensor(z[:, slot, :, :], x_bc[:, t:t + 2, :],
                                        h[layer - 1][:, :].unsqueeze(1).to_broadcast([128, 2, NCOL]),
                                        ALU.mult).then_inc(z_made, 1)
            else:
                k = s - S_L0
                dve.wait_ge(spread, (c + 1) * NBC + k + 1)
                if k == 0:
                    dve.wait_ge(evacuated, (c + 1) * (G1 + 1) + 1)
                    nc.vector.tensor_tensor(z[0:P0, slot, 0, :], bc[0][0:P0, 1, :], x_rep[:, :],
                                            ALU.mult).then_inc(z_made, 1)
                else:
                    nc.vector.tensor_tensor(z[0:P0, slot, :, :], bc[k % 2][0:P0, :, :],
                                            x_rep[:, :].unsqueeze(1).to_broadcast([P0, 2, NCOL]),
                                            ALU.mult).then_inc(z_made, 1)

        def low_part(eng, engine, done, mine, c, s, last):
            if s not in mine:
                return
            eng.wait_ge(zh_made, executed(SPLIT, c, s))
            slot, n = place(s, last), len(tiles_of(s))
            p = P0 if S_L0 <= s < S_L2 else 128
            engine.tensor_tensor(z_l[0:p, slot, 0:n, :], z[0:p, slot, 0:n, :], z_h[0:p, slot, 0:n, :],
                                 ALU.subtract).then_inc(done, 1)

        def dve_sum(dve, c, par, which, last):
            if which == 0:
                dve.wait_ge(acc_drained, 3 * c + 2)
                if not (isinstance(c, int) and c < 2):
                    dve.wait_ge(y_stored[par], 8 * c - 8 * par)
                src = direct01[:, par, :]
            else:
                dve.wait_ge(acc_drained, 3 * c + (3 if last else 4))
                src = direct2[:, :]
            nc.vector.tensor_reduce(y_sum[:, par, which, :], src.rearrange("p (b d) -> p b d", d=D),
                                    AX.X, ALU.add).then_inc(summed, 1)

        @block.vector
        def _(dve):
            nc.vector.memset(x_in[:, :, :], 0.0).then_inc(x_cleared, 1)
            dve.wait_ge(eye_loaded, 16)
            dve.wait_ge(picks_made, 2)
            nc.vector.tensor_copy(pick1[:, :, :].rearrange("p t (f g) -> p (t f) g", g=H),
                                  eye[:, F:2 * F + 1].unsqueeze(2).to_broadcast([XP, F + 1, H])).then_inc(picks_made, 1)
            dve.wait_ge(w0_loaded, 32)
            nc.vector.tensor_tensor(w0_f[:, :, :], w0_f[:, :, :], w0_mirror,
                                    ALU.add).then_inc(w0_summed, 1)
            dve.wait_ge(w_high, 1)
            nc.vector.tensor_tensor(w_l[0][:, :, :], w0_f[:, :, :], w_h[0][:, :, :],
                                    ALU.subtract).then_inc(w_low, 1)
            for s in FIRST_SLOTS:
                dve_product(dve, -1, s, False)
            for s in FIRST_SLOTS:
                low_part(dve, nc.vector, zl_dve, SUB_DVE, -1, s, False)
            for layer in (1, 2):
                dve.wait_ge(w_high, layer + 1)
                nc.vector.tensor_tensor(w_l[layer][:, :, :], w_full[layer], w_h[layer][:, :, :],
                                        ALU.subtract).then_inc(w_low, 1)

            def pair(c, first=False, last=False):
                for par in range(2):
                    end = last and par == 1
                    slots = LAST_SLOTS if end else SLOTS
                    for n, s in enumerate(slots):
                        if end and s == S_L2:
                            for before in slots[n - SUB_LAG:n]:
                                low_part(dve, nc.vector, zl_dve, SUB_DVE, c + par, before, end)
                        dve_product(dve, c + par, s, end)
                        if end and G1 <= n < G1 + SUB_LAG:
                            pass
                        elif n >= SUB_LAG:
                            low_part(dve, nc.vector, zl_dve, SUB_DVE, c + par, slots[n - SUB_LAG], end)
                        elif not (first and par == 0):
                            low_part(dve, nc.vector, zl_dve, SUB_DVE, c + par - 1, SLOTS[n - SUB_LAG], False)
                        if s == DVE_SUM_L2_AT and not (first and par == 0):
                            dve_sum(dve, c + par - 1, (par + 1) % 2, 1, False)
                        if s == DVE_SUM_L1_AT:
                            dve_sum(dve, c + par, par, 0, end)

            pair(0, first=True)
            with dve.Fori(1, NBLK // 2 - 1) as i:
                pair(2 * i)
            pair(NBLK - 2, last=True)
            for s in LAST_SLOTS[-SUB_LAG:]:
                low_part(dve, nc.vector, zl_dve, SUB_DVE, NBLK - 1, s, True)
            dve_sum(dve, NBLK - 1, 1, 1, True)

        def pool_split_x(pool, b, par, before):
            if before is not None:
                pool.wait_ge(zl_pool, before)
            pool.wait_ge(x_high, b + 1)
            nc.gpsimd.tensor_tensor(x_split[64:XP, par, :], x_in[64:XP, par, :], x_split[64:XP, par, :],
                                    ALU.subtract).then_inc(x_low, 1)
            pool.wait_ge(x_low, b + 1)

        @block.gpsimd
        def _(pool):
            pool_split_x(pool, 0, 0, None)
            for s in FIRST_SLOTS:
                low_part(pool, nc.gpsimd, zl_pool, SUB_POOL, -1, s, False)
            pool_split_x(pool, 1, 1, executed(SUB_POOL, -1, S_L2 - 1))

            def pair(c, last=False):
                for par in range(2):
                    end = last and par == 1
                    for s in (LAST_SLOTS if end else SLOTS):
                        low_part(pool, nc.gpsimd, zl_pool, SUB_POOL, c + par, s, end)
                        if s == POOL_X_AT and not last:
                            pool_split_x(pool, c + par + 2, par, executed(SUB_POOL, c + par, s))

            with pool.Fori(0, NBLK // 2 - 1) as i:
                pair(2 * i)
            pair(NBLK - 2, last=True)


def kernel(**inputs):
    import numpy as _np
    import concourse.bacc as _bacc
    from concourse import mybir as _mybir
    from concourse.bass_utils import run_bass_kernel_spmd as _run

    x = _np.asarray(inputs["r_x"])
    x_t = _np.ascontiguousarray(x.transpose(1, 0, 2).reshape(F, B * D))
    w0 = _np.asarray(inputs["L0_rec_W0"]).reshape(F, F, L)
    w0a = _np.zeros((P0, T0, L), w0.dtype)
    w0b = _np.zeros((P0, T0, L), w0.dtype)
    f = _np.arange(F)
    for k in range(20):
        g, t, j = (f + k) % F, k // KS, k % KS
        w0a[j * F:(j + 1) * F, t] = w0[f, g]
        if k:
            w0b[j * F:(j + 1) * F, t] = w0[g, f]
    arrays = {"x_t": x_t, "w0a": w0a, "w0b": w0b}
    for name in ("W1", "W2"):
        w = _np.asarray(inputs["L0_rec_" + name])
        padded = _np.zeros((T1 * 128, L), w.dtype)
        padded[:F * H] = w
        arrays[name] = _np.ascontiguousarray(padded.reshape(T1, 128, L).transpose(1, 0, 2))
    eye = _np.zeros((XP, 2 * F + 1), _np.float32)
    for at in (0, 64):
        eye[at + f, f] = 1
        eye[at + f, F + f] = 1
    arrays["eye"] = eye
    for name in ("b0", "b1", "b2"):
        arrays[name] = _np.ascontiguousarray(inputs["L0_rec_" + name])

    nc = _bacc.Bacc("TRN2", target_bir_lowering=False, num_devices=1)
    args = [nc.dram_tensor("in_" + n, a.shape, _mybir.dt.from_np(a.dtype), kind="ExternalInput").ap()
            for n, a in arrays.items()]
    y_d = nc.dram_tensor("out_y", (2, 128, B), _mybir.dt.float32, kind="ExternalOutput").ap()
    build(nc, *args, y_d)
    r = _run(nc, [{"in_" + n: a for n, a in arrays.items()}], core_ids=[0])
    y = r.results[0]["out_y"]
    rows = _np.concatenate([y[0, H:L], y[0, 0:H], y[1]], axis=0)
    return _np.ascontiguousarray(rows.T)
```

```python
import concourse.bass as bass
from concourse import mybir
from contextlib import ExitStack

F = 39
D = 16
B = 2048
L = 128
H = L // 2
NCOL = 512
BB = NCOL // D
NBLK = B // BB
KS = 3
P0 = KS * F
T0 = 7
K0_LAST = (20 - KS * (T0 - 1)) * F
T1 = (F + 1) // 2
XP = 64 + F

G0, G1 = 4, T1 // 2
SLOTS = list(range(2 * G1 + G0))
S_L0, S_L2 = G1, G1 + G0
LAST_SLOTS = [s for s in SLOTS if not S_L0 <= s < S_L2]
FIRST_SLOTS = [s for s in SLOTS if S_L0 <= s < S_L2]
RING = 6
ZRING = 6
SUB_DVE = [1, 5, 9, 17, 21]
SUB_POOL = [0, 2, 4, 6, 7, 8, 10, 11, 12, 14, 16, 19, 20, 22, 23]
SPLIT = sorted(SUB_DVE + SUB_POOL)
WHOLE = [s for s in SLOTS if s not in SPLIT and not S_L0 <= s < S_L2]
NBC = T0 + T1
SPREAD_AFTER = [10, 11, 12, 15, 15, 18, 19, 22, 24, 25, 27, 27, 28, 30, 32, 36, 36, 38, 40, 42, 43, 44, 45, 48, 50, 53, 56]
SUB_LAG = 2
EVAC_AFTER = [13, 14, 15, 16, 16, 17, 20, 20, 21, 22, 23, 23, 24, 24, 25, 25, 27, 29, 31, 31]
ACT_RELU_L2_AT, ACT_X_AT, ACT_RELU_L1_AT, ACT_RELU_L0_AT = 2, 8, 13, 17
DVE_SUM_L2_AT, DVE_SUM_L1_AT = 6, 22
POOL_X_AT = 14


def executed(slots, c, s):
    first = len([p for p in slots if p in FIRST_SLOTS])
    upto = len([p for p in slots if p <= s])
    if isinstance(c, int) and c == -1:
        return len([p for p in slots if p in FIRST_SLOTS and p <= s])
    skipped = first if isinstance(c, int) and c == NBLK - 1 and s >= S_L2 else 0
    return c * len(slots) + (first + upto - skipped)


def place(s, last, ring=RING):
    return (len(FIRST_SLOTS) + s - (G0 if last and s >= S_L2 else 0)) % ring


def low_after(s):
    after = [p for p in SUB_DVE if p > s] + [SUB_DVE[0] + len(SLOTS)]
    return min(s + SUB_LAG, after[0] - 1)


def earlier(c, s, n, last):
    if isinstance(c, int) and c == -1:
        return (c, s - n) if s - n >= S_L0 else None
    order = LAST_SLOTS if last else SLOTS
    at = order.index(s) - n
    if at >= 0:
        return c, order[at]
    if isinstance(c, int) and c == 0:
        return (-1, FIRST_SLOTS[at]) if -at <= len(FIRST_SLOTS) else None
    return c - 1, SLOTS[at]


def tiles_of(s):
    if s < S_L0:
        return [2 * s, 2 * s + 1]
    if s < S_L2:
        g = s - S_L0
        return [0] if g == 0 else [2 * g - 1, 2 * g]
    return [2 * (s - S_L2), 2 * (s - S_L2) + 1]


def build(nc, x_t, w0a_d, w0b_d, w1_d, w2_d, eye_d, b0_d, b1_d, b2_d, y_d):
    fp32 = mybir.dt.float32
    f32r = mybir.dt.float32r
    ALU = mybir.AluOpType
    ACT = mybir.ActivationFunctionType
    AX = mybir.AxisListType

    with ExitStack() as ctx:
        def sb(name, shape, dt=fp32):
            return ctx.enter_context(nc.sbuf_tensor(name, shape, dt))

        def sem(name):
            return ctx.enter_context(nc.semaphore(name))

        w0_f = sb("w0_f", [P0, T0, L])
        w12_f = sb("w12_f", [128, len(WHOLE), 2, L])
        w_h = [sb("w0_h", [P0, T0, L], f32r), sb("w1_h", [128, T1, L], f32r), sb("w2_h", [128, T1, L], f32r)]
        w_l = [sb("w0_l", [P0, T0, L], f32r), sb("w1_l", [128, T1, L], f32r), sb("w2_l", [128, T1, L], f32r)]
        eye = sb("eye", [XP, 2 * F + 1])
        pick0 = sb("pick0", [XP, T0, P0], f32r)
        pick1 = sb("pick1", [XP, T1, 128], f32r)
        bias = sb("bias", [128, 3])

        x_in = sb("x_in", [XP, 2, NCOL])
        x_split = sb("x_split", [XP, 2, NCOL], f32r)
        x_rep = sb("x_rep", [P0, 2, NCOL])
        x_bc = sb("x_bc", [128, T1, NCOL])
        stage = x_bc[:, :, :].rearrange("p t n -> p (t n)")
        at0, at1, at2 = (T1 - 12) * NCOL, (T1 - 10) * NCOL, (T1 - 5) * NCOL
        w0_mirror = stage[0:P0, at0:at0 + T0 * L].rearrange("p (t l) -> p t l", l=L)
        w_full = [w0_f[:, :, :],
                  stage[:, at1:at1 + T1 * L].rearrange("p (t l) -> p t l", l=L),
                  stage[:, at2:at2 + T1 * L].rearrange("p (t l) -> p t l", l=L)]
        z = sb("z", [128, ZRING, 2, NCOL])
        z_h = sb("z_h", [128, RING, 2, NCOL], f32r)
        z_l = sb("z_l", [128, RING, 2, NCOL], f32r)
        direct01 = sb("direct01", [128, 2, NCOL])
        direct2 = sb("direct2", [128, NCOL])
        y_sum = sb("y_sum", [128, 2, 2, BB])

        acc = [ctx.enter_context(nc.psum_tensor(f"acc{i}", [128, NCOL], fp32)) for i in range(2)]
        h = [ctx.enter_context(nc.psum_tensor(f"h{i}", [128, NCOL], fp32)) for i in range(2)]
        bc = ctx.enter_context(nc.psum_tensor("bc", [128, 2, NCOL], fp32))
        z_psum = ctx.enter_context(nc.psum_tensor("z_psum", [128, 2, NCOL], fp32))

        w0_loaded, w1_loaded, w2_loaded = sem("w0_loaded"), sem("w1_loaded"), sem("w2_loaded")
        w12_whole_loaded, eye_loaded, bias_loaded = sem("w12_whole_loaded"), sem("eye_loaded"), sem("bias_loaded")
        x_cleared = sem("x_cleared")
        w0_summed = sem("w0_summed")
        w_high = sem("w_high")
        w_low = sem("w_low")
        picks_made = sem("picks_made")
        x_loaded = [sem("x_loaded_even"), sem("x_loaded_odd")]
        x_rep_loaded = [sem("x_rep_loaded_even"), sem("x_rep_loaded_odd")]
        x_high = sem("x_high")
        x_low = sem("x_low")
        spread = sem("spread")
        evacuated = sem("evacuated")
        h_ready = sem("h_ready")
        acc_drained = sem("acc_drained")
        z_made = sem("z_made")
        zh_made = sem("zh_made")
        zl_dve = sem("zl_dve")
        zl_pool = sem("zl_pool")
        contracted = sem("contracted")
        summed = sem("summed")
        y_stored = [sem("y_stored_even"), sem("y_stored_odd")]

        block = ctx.enter_context(nc.Block())

        def z_of(s, last):
            return z_psum[:, :, :] if s in SUB_DVE else z[:, place(s, last, ZRING), :, :]

        def load_x(eng, b, par):
            if not (isinstance(b, int) and b < 2):
                eng.wait_ge(x_low, b - 1)
            src = x_t[:, bass.ds(b * NCOL, NCOL)]
            eng.dma_start(x_in[0:F, par, :], src).then_inc(x_loaded[par], 16)
            eng.dma_start(x_in[64:XP, par, :], src).then_inc(x_loaded[par], 16)
            if not (isinstance(b, int) and b < 2):
                eng.wait_ge(z_made, executed(SLOTS, b - 3, S_L2 - 1))
            for k in range(KS):
                eng.dma_start(x_rep[k * F:(k + 1) * F, par, :], src).then_inc(x_rep_loaded[par], 16)

        def store_y(eng, c, par):
            eng.wait_ge(summed, 2 * c + 2)
            dst = y_d[:, :, bass.ds(c * BB, BB)].rearrange("a p b -> p a b")
            eng.dma_start(dst, y_sum[:, par, :, :]).then_inc(y_stored[par], 16)

        @block.sync
        def _(sp):
            sp.dma_start(eye[:, :], eye_d).then_inc(eye_loaded, 16)
            sp.wait_ge(x_cleared, 1)
            load_x(sp, 0, 0)
            load_x(sp, 1, 1)
            sp.dma_start(w_full[1], w1_d).then_inc(w1_loaded, 16)
            for n, s in enumerate(WHOLE):
                w_d, t = (w1_d if s < S_L0 else w2_d), tiles_of(s)[0]
                sp.dma_start(w12_f[:, n, :, :], w_d[:, t:t + 2, :]).then_inc(w12_whole_loaded, 16)
            sp.dma_start(w_full[2], w2_d).then_inc(w2_loaded, 16)

            def pair(c, last=False):
                for par in range(2):
                    if not last:
                        load_x(sp, c + par + 2, par)
                    store_y(sp, c + par, par)

            pair(0)
            with sp.Fori(1, NBLK // 2 - 1) as i:
                pair(2 * i)
            pair(NBLK - 2, last=True)
            sp.wait_ge(y_stored[0], 16 * (NBLK // 2))
            sp.wait_ge(y_stored[1], 16 * (NBLK // 2))

        def pe_spread(pe, u, c, par):
            bank = (u + 1) % 2
            if u == 0:
                pe.wait_ge(x_low, c + 2)
            if u < 2:
                if not (isinstance(c, int) and c == -1):
                    pe.wait_ge(evacuated, (c + 1) * T1 - u)
            elif u <= T0 + 1:
                pe.wait_ge(z_made, executed(SLOTS, c, S_L0 + (u + 1) // 2 - 1))
            else:
                pe.wait_ge(evacuated, (c + 1) * T1 + u - T0 - 1)
            xs = x_split[:, par, :]
            if u < T0:
                m = nc.tensor.matmul(bc[0:P0, bank, :], pick0[:, u, :], xs, start=True, stop=True)
            else:
                m = nc.tensor.matmul(bc[:, bank, :], pick1[:, u - T0, :], xs, start=True, stop=True)
            m.then_inc(spread, 1)

        def pe_contract(pe, c, par, s, last, between):
            layer = 1 if s < S_L0 else 0 if s < S_L2 else 2
            stage = 3 * c + (1 if layer == 1 else 2 if layer == 0 or last else 3)
            a = acc[(par + (1 if layer == 1 else 0 if layer == 0 or last else 1)) % 2]
            tiles = tiles_of(s)
            n_tiles = T0 if layer == 0 else T1
            if tiles[0] == 0 and not (isinstance(stage, int) and stage < 2):
                pe.wait_ge(acc_drained, stage - 1)
            slot = place(s, last)
            kp = [K0_LAST if layer == 0 and t == T0 - 1 else P0 if layer == 0 else 128 for t in tiles]
            if s not in SPLIT:
                pe.wait_ge(z_made, executed(SLOTS, c, s))
                for j, t in enumerate(tiles):
                    w = w0_f[0:kp[j], t, :] if layer == 0 else w12_f[:, WHOLE.index(s), j, :]
                    if j == 1:
                        between(2 * s)
                    m = nc.tensor.matmul(a[:, :], w, z_of(s, last)[0:kp[j], j, :],
                                         start=(t == 0), stop=(t == n_tiles - 1))
                if len(tiles) == 1:
                    between(2 * s)
            else:
                pe.wait_ge(zh_made, executed(SPLIT, c, s))
                for j, t in enumerate(tiles):
                    for w in (w_h, w_l):
                        m = nc.tensor.matmul(a[:, :], w[layer][0:kp[j], t, :], z_h[0:kp[j], slot, j, :],
                                             start=(t == 0 and w is w_h), stop=False)
                between(2 * s)
                if s in SUB_DVE:
                    pe.wait_ge(zl_dve, executed(SUB_DVE, c, s))
                else:
                    pe.wait_ge(zl_pool, executed(SUB_POOL, c, s))
                for j, t in enumerate(tiles):
                    m = nc.tensor.matmul(a[:, :], w_h[layer][0:kp[j], t, :], z_l[0:kp[j], slot, j, :],
                                         start=False, stop=(t == n_tiles - 1))
            m.then_inc(contracted, 1)
            between(2 * s + 1)

        @block.tensor
        def _(pe):
            pe.wait_ge(picks_made, 1)
            for u in range(T0):
                pe_spread(pe, u, -1, 0)
            pe.wait_ge(w_high, 1)
            pe.wait_ge(w_low, 1)
            for s in FIRST_SLOTS:
                pe_contract(pe, -1, 1, s, False, lambda half: None)
            pe.wait_ge(picks_made, 2)
            for u in range(T0, NBC):
                pe_spread(pe, u, -1, 0)

            def pair(c, first=False, last=False):
                for par in range(2):
                    end = last and par == 1
                    for s in (LAST_SLOTS if end else SLOTS):
                        if first and par == 0 and s == 0:
                            pe.wait_ge(w12_whole_loaded, 16 * len(WHOLE))
                        if first and par == 0 and s in (0, S_L2):
                            pe.wait_ge(w_high, 2 if s == 0 else 3)
                            pe.wait_ge(w_low, 2 if s == 0 else 3)

                        def spreads(half):
                            for u in range(NBC):
                                if SPREAD_AFTER[u] == half + 2 * len(SLOTS) and not (first and par == 0):
                                    pe_spread(pe, u, c + par - 1, par)
                            for u in range(NBC):
                                if SPREAD_AFTER[u] == half and not end:
                                    pe_spread(pe, u, c + par, (par + 1) % 2)

                        pe_contract(pe, c + par, par, s, end, spreads)

            pair(0, first=True)
            with pe.Fori(1, NBLK // 2 - 1) as i:
                pair(2 * i)
            pair(NBLK - 2, last=True)

        def act_split_x(act, b, par, used):
            act.wait_ge(x_loaded[par], 32 * ((b - par) // 2 + 1) if isinstance(b, int) else used)
            nc.scalar.activation(x_split[:, par, :], x_in[:, par, :], ACT.Copy).then_inc(x_high, 1)

        def act_evac(act, c, t):
            act.wait_ge(spread, (c + 1) * NBC + T0 + 1 + t)
            if not (isinstance(c, int) and c == -1):
                act.wait_ge(z_made, executed(SLOTS, c, S_L2 + t // 2))
            elif t == T1 - 12:
                act.wait_ge(w_low, 3)
            nc.scalar.activation(x_bc[:, t, :], bc[:, t % 2, :], ACT.Copy).then_inc(evacuated, 1)

        def act_round(act, c, s, last):
            if s not in SPLIT:
                return
            count = executed(SLOTS, c, s)
            act.wait_ge(z_made, count)
            if not (isinstance(count, int) and count <= RING):
                act.wait_ge(contracted, count - RING)
            slot, n = place(s, last), len(tiles_of(s))
            p = P0 if S_L0 <= s < S_L2 else 128
            nc.scalar.activation(z_h[0:p, slot, 0:n, :], z_of(s, last)[0:p, 0:n, :], ACT.Copy).then_inc(zh_made, 1)

        def act_relu(act, c, par, layer, last):
            stage = {1: 1, 0: 2, 2: 2 if last else 3}[layer]
            a = acc[(par + stage) % 2]
            end = {1: S_L0 - 1, 0: S_L2 - 1, 2: SLOTS[-1]}[layer]
            act.wait_ge(contracted, executed(SLOTS, c, end))
            blk = (par + 1) % 2 if layer == 0 else par
            if layer < 2:
                for half in range(2):
                    nc.scalar.activation(h[layer][H * half:H * half + H, :], a[0:H, :], ACT.Relu,
                                         bias=bias[0:H, layer:layer + 1]).then_inc(h_ready, 1)
                dst = direct01[H:L, blk, :] if layer == 0 else direct01[0:H, blk, :]
                b = c + 1 if layer == 0 else c
                if not (isinstance(b, int) and b < 2):
                    act.wait_ge(summed, 2 * b - 3)
                nc.scalar.activation(dst, a[H:L, :], ACT.Relu, bias=bias[H:L, layer:layer + 1]).then_inc(acc_drained, 1)
            else:
                if not (isinstance(c, int) and c == 0):
                    act.wait_ge(summed, 2 * c)
                nc.scalar.activation(direct2[:, :], a[:, :], ACT.Relu, bias=bias[:, 2:3]).then_inc(acc_drained, 1)

        @block.scalar
        def _(act):
            act.dma_start(w0_f[:, :, :], w0a_d).then_inc(w0_loaded, 16)
            act.dma_start(w0_mirror, w0b_d).then_inc(w0_loaded, 16)
            for n, b_d in enumerate((b0_d, b1_d, b2_d)):
                act.dma_start(bias[:, n:n + 1], b_d.rearrange("(p a) -> p a", a=1)).then_inc(bias_loaded, 16)
            act.wait_ge(eye_loaded, 16)
            nc.scalar.activation(pick0[:, :, :].rearrange("p t (k f) -> p (t k) f", f=F),
                                 bass.AP(tensor=eye, offset=0, ap=[[2 * F + 1, XP], [1, T0 * KS], [1, F]]),
                                 ACT.Copy).then_inc(picks_made, 1)
            act_split_x(act, 0, 0, None)
            act.wait_ge(w0_summed, 1)
            nc.scalar.activation(w_h[0][:, :, :], w_full[0], ACT.Copy).then_inc(w_high, 1)
            for s in FIRST_SLOTS:
                act_round(act, -1, s, False)
            act_split_x(act, 1, 1, None)
            act.wait_ge(w1_loaded, 16)
            nc.scalar.activation(w_h[1][:, :, :], w_full[1], ACT.Copy).then_inc(w_high, 1)
            act.wait_ge(w2_loaded, 16)
            nc.scalar.activation(w_h[2][:, :, :], w_full[2], ACT.Copy).then_inc(w_high, 1)
            act.wait_ge(bias_loaded, 48)
            act_relu(act, -1, 1, 0, False)
            for t in range(T1):
                act_evac(act, -1, t)

            def pair(c, first=False, last=False):
                for par in range(2):
                    end = last and par == 1
                    for s in (LAST_SLOTS if end else SLOTS):
                        act_round(act, c + par, s, end)
                        if s == ACT_RELU_L2_AT and not (first and par == 0):
                            act_relu(act, c + par - 1, (par + 1) % 2, 2, False)
                        if s == ACT_X_AT and not last:
                            act_split_x(act, c + par + 2, par, 16 * c + 64)
                        if s == (S_L0 - 1 if end else ACT_RELU_L1_AT):
                            act_relu(act, c + par, par, 1, end)
                        if s == ACT_RELU_L0_AT and not end:
                            act_relu(act, c + par, par, 0, False)
                        for t in range(T1):
                            if EVAC_AFTER[t] == s + len(SLOTS) and not (first and par == 0):
                                act_evac(act, c + par - 1, t)
                        for t in range(T1):
                            if EVAC_AFTER[t] == s and not end:
                                act_evac(act, c + par, t)

            pair(0, first=True)
            with act.Fori(1, NBLK // 2 - 1) as i:
                pair(2 * i)
            pair(NBLK - 2, last=True)
            act_relu(act, NBLK - 1, 1, 2, True)

        def dve_product(dve, c, par, s, last):
            out = z_of(s, last)
            if s in SUB_DVE and not (isinstance(c, int) and executed(SUB_DVE, c, s) == 1):
                dve.wait_ge(zl_dve, executed(SUB_DVE, c, s) - 1)
            rounds = 1
            before = earlier(c, s, ZRING, last)
            while before and before[1] in SUB_DVE:
                rounds += 1
                before = earlier(c, s, rounds * ZRING, last)
            if s not in SUB_DVE and before:
                if before[1] in SUB_POOL:
                    dve.wait_ge(zl_pool, executed(SUB_POOL, *before))
                elif before[1] not in SPLIT:
                    dve.wait_ge(contracted, executed(SLOTS, *before))
            if s < S_L0 or s >= S_L2:
                layer = 1 if s < S_L0 else 2
                t = tiles_of(s)[0]
                if layer == 1:
                    dve.wait_ge(evacuated, c * T1 + 2 * (s + 1))
                if t == 0:
                    dve.wait_ge(h_ready, 4 * c + 2 if layer == 1 else 4 * c + 4)
                nc.vector.tensor_tensor(out, x_bc[:, t:t + 2, :],
                                        h[layer - 1][:, :].unsqueeze(1).to_broadcast([128, 2, NCOL]),
                                        ALU.mult).then_inc(z_made, 1)
            else:
                k = s - S_L0
                dve.wait_ge(spread, (c + 1) * NBC + 2 * k + 1)
                if k == 0:
                    dve.wait_ge(x_rep_loaded[(par + 1) % 2], 24 * (c - par) + 48 + 48 * par)
                    nc.vector.tensor_tensor(out[0:P0, 0, :], bc[0:P0, 1, :], x_rep[:, (par + 1) % 2, :],
                                            ALU.mult).then_inc(z_made, 1)
                else:
                    nc.vector.tensor_tensor(out[0:P0, :, :], bc[0:P0, :, :],
                                            x_rep[:, (par + 1) % 2, :].unsqueeze(1).to_broadcast([P0, 2, NCOL]),
                                            ALU.mult).then_inc(z_made, 1)

        def low_part(eng, engine, done, mine, c, s, last):
            if s not in mine:
                return
            eng.wait_ge(zh_made, executed(SPLIT, c, s))
            slot, n = place(s, last), len(tiles_of(s))
            p = P0 if S_L0 <= s < S_L2 else 128
            engine.tensor_tensor(z_l[0:p, slot, 0:n, :], z_of(s, last)[0:p, 0:n, :], z_h[0:p, slot, 0:n, :],
                                 ALU.subtract).then_inc(done, 1)

        def dve_sum(dve, c, par, which, last):
            if which == 0:
                dve.wait_ge(acc_drained, 3 * c + 2)
                if not (isinstance(c, int) and c < 2):
                    dve.wait_ge(y_stored[par], 8 * c - 8 * par)
                src = direct01[:, par, :]
            else:
                dve.wait_ge(acc_drained, 3 * c + (3 if last else 4))
                src = direct2[:, :]
            nc.vector.tensor_reduce(y_sum[:, par, which, :], src.rearrange("p (b d) -> p b d", d=D),
                                    AX.X, ALU.add).then_inc(summed, 1)

        @block.vector
        def _(dve):
            nc.vector.memset(x_in[:, :, :], 0.0).then_inc(x_cleared, 1)
            dve.wait_ge(eye_loaded, 16)
            dve.wait_ge(picks_made, 1)
            nc.vector.tensor_copy(pick1[:, :, :].rearrange("p t (f g) -> p (t f) g", g=H),
                                  eye[:, F:2 * F + 1].unsqueeze(2).to_broadcast([XP, F + 1, H])).then_inc(picks_made, 1)
            dve.wait_ge(w0_loaded, 32)
            nc.vector.tensor_tensor(w0_f[:, :, :], w0_f[:, :, :], w0_mirror,
                                    ALU.add).then_inc(w0_summed, 1)
            dve.wait_ge(w_high, 1)
            nc.vector.tensor_tensor(w_l[0][:, :, :], w0_f[:, :, :], w_h[0][:, :, :],
                                    ALU.subtract).then_inc(w_low, 1)
            for s in FIRST_SLOTS:
                dve_product(dve, -1, 1, s, False)
                low_part(dve, nc.vector, zl_dve, SUB_DVE, -1, s, False)
            for layer in (1, 2):
                dve.wait_ge(w_high, layer + 1)
                nc.vector.tensor_tensor(w_l[layer][:, :, :], w_full[layer], w_h[layer][:, :, :],
                                        ALU.subtract).then_inc(w_low, 1)

            def pair(c, first=False, last=False):
                for par in range(2):
                    end = last and par == 1
                    slots = LAST_SLOTS if end else SLOTS
                    for s in slots:
                        if end and s == S_L2:
                            for before in SUB_DVE:
                                if before < S_L0 <= low_after(before) < S_L2:
                                    low_part(dve, nc.vector, zl_dve, SUB_DVE, c + par, before, end)
                        dve_product(dve, c + par, par, s, end)
                        for before in SUB_DVE:
                            if low_after(before) % len(SLOTS) == s:
                                if before <= s and before in slots:
                                    low_part(dve, nc.vector, zl_dve, SUB_DVE, c + par, before, end)
                                elif before > s and not (first and par == 0):
                                    low_part(dve, nc.vector, zl_dve, SUB_DVE, c + par - 1, before, False)
                        if s == DVE_SUM_L2_AT and not (first and par == 0):
                            dve_sum(dve, c + par - 1, (par + 1) % 2, 1, False)
                        if s == DVE_SUM_L1_AT:
                            dve_sum(dve, c + par, par, 0, end)

            pair(0, first=True)
            with dve.Fori(1, NBLK // 2 - 1) as i:
                pair(2 * i)
            pair(NBLK - 2, last=True)
            for s in SUB_DVE:
                if low_after(s) >= len(SLOTS):
                    low_part(dve, nc.vector, zl_dve, SUB_DVE, NBLK - 1, s, True)
            dve_sum(dve, NBLK - 1, 1, 1, True)

        def pool_split_x(pool, b, par, before):
            if before is not None:
                pool.wait_ge(zl_pool, before)
            pool.wait_ge(x_high, b + 1)
            nc.gpsimd.tensor_tensor(x_split[64:XP, par, :], x_in[64:XP, par, :], x_split[64:XP, par, :],
                                    ALU.subtract).then_inc(x_low, 1)
            pool.wait_ge(x_low, b + 1)

        @block.gpsimd
        def _(pool):
            pool_split_x(pool, 0, 0, None)
            for s in FIRST_SLOTS:
                low_part(pool, nc.gpsimd, zl_pool, SUB_POOL, -1, s, False)
            pool_split_x(pool, 1, 1, executed(SUB_POOL, -1, S_L2 - 1))

            def pair(c, last=False):
                for par in range(2):
                    end = last and par == 1
                    for s in (LAST_SLOTS if end else SLOTS):
                        low_part(pool, nc.gpsimd, zl_pool, SUB_POOL, c + par, s, end)
                        if s == POOL_X_AT and not last:
                            pool_split_x(pool, c + par + 2, par, executed(SUB_POOL, c + par, s))

            with pool.Fori(0, NBLK // 2 - 1) as i:
                pair(2 * i)
            pair(NBLK - 2, last=True)


def kernel(**inputs):
    import numpy as _np
    import concourse.bacc as _bacc
    from concourse import mybir as _mybir
    from concourse.bass_utils import run_bass_kernel_spmd as _run

    x = _np.asarray(inputs["r_x"])
    x_t = _np.ascontiguousarray(x.transpose(1, 0, 2).reshape(F, B * D))
    w0 = _np.asarray(inputs["L0_rec_W0"]).reshape(F, F, L)
    w0a = _np.zeros((P0, T0, L), w0.dtype)
    w0b = _np.zeros((P0, T0, L), w0.dtype)
    f = _np.arange(F)
    for k in range(20):
        g, t, j = (f + k) % F, k // KS, k % KS
        w0a[j * F:(j + 1) * F, t] = w0[f, g]
        if k:
            w0b[j * F:(j + 1) * F, t] = w0[g, f]
    arrays = {"x_t": x_t, "w0a": w0a, "w0b": w0b}
    for name in ("W1", "W2"):
        w = _np.asarray(inputs["L0_rec_" + name])
        padded = _np.zeros((T1 * 128, L), w.dtype)
        padded[:F * H] = w
        arrays[name] = _np.ascontiguousarray(padded.reshape(T1, 128, L).transpose(1, 0, 2))
    eye = _np.zeros((XP, 2 * F + 1), _np.float32)
    for at in (0, 64):
        eye[at + f, f] = 1
        eye[at + f, F + f] = 1
    arrays["eye"] = eye
    for name in ("b0", "b1", "b2"):
        arrays[name] = _np.ascontiguousarray(inputs["L0_rec_" + name])

    nc = _bacc.Bacc("TRN2", target_bir_lowering=False, num_devices=1)
    args = [nc.dram_tensor("in_" + n, a.shape, _mybir.dt.from_np(a.dtype), kind="ExternalInput").ap()
            for n, a in arrays.items()]
    y_d = nc.dram_tensor("out_y", (2, 128, B), _mybir.dt.float32, kind="ExternalOutput").ap()
    build(nc, *args, y_d)
    r = _run(nc, [{"in_" + n: a for n, a in arrays.items()}], core_ids=[0])
    y = r.results[0]["out_y"]
    rows = _np.concatenate([y[0, H:L], y[0, 0:H], y[1]], axis=0)
    return _np.ascontiguousarray(rows.T)
```
